# Optimizing a Trainium2 kernel written in Bass

```python
import numpy as np
import jax
import jax.numpy as jnp

def _softmax(x, axis=-1):
    return jax.nn.softmax(x, axis=axis)

def _gelu(x):
    return jax.nn.gelu(x, approximate=True)

def _silu(x):
    return jax.nn.silu(x)

def _sigmoid(x):
    return jax.nn.sigmoid(x)

def _layernorm(x, axis=-1, eps=1e-05):
    m = jnp.mean(x, axis=axis, keepdims=True)
    v = jnp.var(x, axis=axis, keepdims=True)
    return (x - m) / jnp.sqrt(v + eps)

def _scatter_add(tgt, idx, src, axis=0):
    return tgt.at[idx].add(src)

def _segment_sum(src, seg, n):
    return jax.ops.segment_sum(src, seg, n)
kernel_name = 'mk_dlrm_tower_d1_rec_r8_1a0ced'

def setup_inputs(seed: int=0):
    np.random.seed(seed)
    _w = jnp.asarray

    def _rec_inputs():
        import jax
        import jax.numpy as jnp
        _tk = jax.random.key(seed)
        dense_ctx = jax.random.normal(jax.random.fold_in(_tk, 190), (512, 16), jnp.float32)
        ids = jnp.stack([jax.random.randint(jax.random.fold_in(_tk, 200 + f), (512,), 0, v, jnp.int32) for f, v in enumerate([125000, 1250, 12500, 1000, 1250, 1000, 1000, 1000, 1250, 125000, 1250, 1250, 1000, 1250, 125000, 12500, 125000, 125000, 1250, 1000, 1250, 12500, 12500, 12500, 1250, 1250, 1000, 12500, 1000, 1250, 125000, 125000, 1250, 1000, 1250, 1250, 1250, 1000, 1250, 1250])], axis=1)
        tbl_0 = 0.05 * jax.random.normal(jax.random.fold_in(_tk, 500 + 0), (125000, 32), jnp.float32)
        tbl_1 = 0.05 * jax.random.normal(jax.random.fold_in(_tk, 500 + 1), (1250, 32), jnp.float32)
        tbl_2 = 0.05 * jax.random.normal(jax.random.fold_in(_tk, 500 + 2), (12500, 32), jnp.float32)
        tbl_3 = 0.05 * jax.random.normal(jax.random.fold_in(_tk, 500 + 3), (1000, 32), jnp.float32)
        tbl_4 = 0.05 * jax.random.normal(jax.random.fold_in(_tk, 500 + 4), (1250, 32), jnp.float32)
        tbl_5 = 0.05 * jax.random.normal(jax.random.fold_in(_tk, 500 + 5), (1000, 32), jnp.float32)
        tbl_6 = 0.05 * jax.random.normal(jax.random.fold_in(_tk, 500 + 6), (1000, 32), jnp.float32)
        tbl_7 = 0.05 * jax.random.normal(jax.random.fold_in(_tk, 500 + 7), (1000, 32), jnp.float32)
        tbl_8 = 0.05 * jax.random.normal(jax.random.fold_in(_tk, 500 + 8), (1250, 32), jnp.float32)
        tbl_9 = 0.05 * jax.random.normal(jax.random.fold_in(_tk, 500 + 9), (125000, 32), jnp.float32)
        tbl_10 = 0.05 * jax.random.normal(jax.random.fold_in(_tk, 500 + 10), (1250, 32), jnp.float32)
        tbl_11 = 0.05 * jax.random.normal(jax.random.fold_in(_tk, 500 + 11), (1250, 32), jnp.float32)
        tbl_12 = 0.05 * jax.random.normal(jax.random.fold_in(_tk, 500 + 12), (1000, 32), jnp.float32)
        tbl_13 = 0.05 * jax.random.normal(jax.random.fold_in(_tk, 500 + 13), (1250, 32), jnp.float32)
        tbl_14 = 0.05 * jax.random.normal(jax.random.fold_in(_tk, 500 + 14), (125000, 32), jnp.float32)
        tbl_15 = 0.05 * jax.random.normal(jax.random.fold_in(_tk, 500 + 15), (12500, 32), jnp.float32)
        tbl_16 = 0.05 * jax.random.normal(jax.random.fold_in(_tk, 500 + 16), (125000, 32), jnp.float32)
        tbl_17 = 0.05 * jax.random.normal(jax.random.fold_in(_tk, 500 + 17), (125000, 32), jnp.float32)
        tbl_18 = 0.05 * jax.random.normal(jax.random.fold_in(_tk, 500 + 18), (1250, 32), jnp.float32)
        tbl_19 = 0.05 * jax.random.normal(jax.random.fold_in(_tk, 500 + 19), (1000, 32), jnp.float32)
        tbl_20 = 0.05 * jax.random.normal(jax.random.fold_in(_tk, 500 + 20), (1250, 32), jnp.float32)
        tbl_21 = 0.05 * jax.random.normal(jax.random.fold_in(_tk, 500 + 21), (12500, 32), jnp.float32)
        tbl_22 = 0.05 * jax.random.normal(jax.random.fold_in(_tk, 500 + 22), (12500, 32), jnp.float32)
        tbl_23 = 0.05 * jax.random.normal(jax.random.fold_in(_tk, 500 + 23), (12500, 32), jnp.float32)
        tbl_24 = 0.05 * jax.random.normal(jax.random.fold_in(_tk, 500 + 24), (1250, 32), jnp.float32)
        tbl_25 = 0.05 * jax.random.normal(jax.random.fold_in(_tk, 500 + 25), (1250, 32), jnp.float32)
        tbl_26 = 0.05 * jax.random.normal(jax.random.fold_in(_tk, 500 + 26), (1000, 32), jnp.float32)
        tbl_27 = 0.05 * jax.random.normal(jax.random.fold_in(_tk, 500 + 27), (12500, 32), jnp.float32)
        tbl_28 = 0.05 * jax.random.normal(jax.random.fold_in(_tk, 500 + 28), (1000, 32), jnp.float32)
        tbl_29 = 0.05 * jax.random.normal(jax.random.fold_in(_tk, 500 + 29), (1250, 32), jnp.float32)
        tbl_30 = 0.05 * jax.random.normal(jax.random.fold_in(_tk, 500 + 30), (125000, 32), jnp.float32)
        tbl_31 = 0.05 * jax.random.normal(jax.random.fold_in(_tk, 500 + 31), (125000, 32), jnp.float32)
        tbl_32 = 0.05 * jax.random.normal(jax.random.fold_in(_tk, 500 + 32), (1250, 32), jnp.float32)
        tbl_33 = 0.05 * jax.random.normal(jax.random.fold_in(_tk, 500 + 33), (1000, 32), jnp.float32)
        tbl_34 = 0.05 * jax.random.normal(jax.random.fold_in(_tk, 500 + 34), (1250, 32), jnp.float32)
        tbl_35 = 0.05 * jax.random.normal(jax.random.fold_in(_tk, 500 + 35), (1250, 32), jnp.float32)
        tbl_36 = 0.05 * jax.random.normal(jax.random.fold_in(_tk, 500 + 36), (1250, 32), jnp.float32)
        tbl_37 = 0.05 * jax.random.normal(jax.random.fold_in(_tk, 500 + 37), (1000, 32), jnp.float32)
        tbl_38 = 0.05 * jax.random.normal(jax.random.fold_in(_tk, 500 + 38), (1250, 32), jnp.float32)
        tbl_39 = 0.05 * jax.random.normal(jax.random.fold_in(_tk, 500 + 39), (1250, 32), jnp.float32)
        _rk = jax.random.fold_in(_tk, 7)
        W_top1 = 0.049029 * jax.random.normal(jax.random.fold_in(_tk, 801), (416, 512), jnp.float32)
        W_top2 = 0.0441942 * jax.random.normal(jax.random.fold_in(_tk, 802), (512, 256), jnp.float32)
        W_top3 = 0.0625 * jax.random.normal(jax.random.fold_in(_tk, 803), (256, 1), jnp.float32)
        b_top1 = jnp.zeros((512,), jnp.float32)
        b_top2 = jnp.zeros((256,), jnp.float32)
        return (dense_ctx, ids, tbl_0, tbl_1, tbl_2, tbl_3, tbl_4, tbl_5, tbl_6, tbl_7, tbl_8, tbl_9, tbl_10, tbl_11, tbl_12, tbl_13, tbl_14, tbl_15, tbl_16, tbl_17, tbl_18, tbl_19, tbl_20, tbl_21, tbl_22, tbl_23, tbl_24, tbl_25, tbl_26, tbl_27, tbl_28, tbl_29, tbl_30, tbl_31, tbl_32, tbl_33, tbl_34, tbl_35, tbl_36, tbl_37, tbl_38, tbl_39, W_top1, b_top1, W_top2, b_top2, W_top3)
    dense_ctx, ids, tbl_0, tbl_1, tbl_2, tbl_3, tbl_4, tbl_5, tbl_6, tbl_7, tbl_8, tbl_9, tbl_10, tbl_11, tbl_12, tbl_13, tbl_14, tbl_15, tbl_16, tbl_17, tbl_18, tbl_19, tbl_20, tbl_21, tbl_22, tbl_23, tbl_24, tbl_25, tbl_26, tbl_27, tbl_28, tbl_29, tbl_30, tbl_31, tbl_32, tbl_33, tbl_34, tbl_35, tbl_36, tbl_37, tbl_38, tbl_39, W_top1, b_top1, W_top2, b_top2, W_top3 = _rec_inputs()

    def _L0_rec_setup():
        import jax, jax.numpy as jnp
        import numpy as np
        LAYER_SIZES = [200, 200, 200]
        key = jax.random.key(seed)
        ks = jax.random.split(key, 7)
        B, F, D = (256, 40, 32)
        field_nums = [F, 100, 100]
        inp = {'inputs': jax.random.normal(ks[0], (B, F, D), dtype=jnp.float32)}
        for i, size in enumerate(LAYER_SIZES):
            fan_in = field_nums[i] * F
            inp[f'W{i}'] = jax.random.normal(ks[1 + 2 * i], (size, fan_in), dtype=jnp.float32) * (1.0 / np.sqrt(fan_in))
            inp[f'b{i}'] = jnp.zeros((size,), dtype=jnp.float32)
        return inp
    _L0_rec_all = _L0_rec_setup()
    _L0_rec_in = {k: v for k, v in _L0_rec_all.items() if k in ('W0', 'b0', 'W1', 'b1', 'W2', 'b2')}
    del _L0_rec_all
    return {'dense_ctx': dense_ctx, 'ids': ids, 'tbl_0': tbl_0, 'tbl_1': tbl_1, 'tbl_2': tbl_2, 'tbl_3': tbl_3, 'tbl_4': tbl_4, 'tbl_5': tbl_5, 'tbl_6': tbl_6, 'tbl_7': tbl_7, 'tbl_8': tbl_8, 'tbl_9': tbl_9, 'tbl_10': tbl_10, 'tbl_11': tbl_11, 'tbl_12': tbl_12, 'tbl_13': tbl_13, 'tbl_14': tbl_14, 'tbl_15': tbl_15, 'tbl_16': tbl_16, 'tbl_17': tbl_17, 'tbl_18': tbl_18, 'tbl_19': tbl_19, 'tbl_20': tbl_20, 'tbl_21': tbl_21, 'tbl_22': tbl_22, 'tbl_23': tbl_23, 'tbl_24': tbl_24, 'tbl_25': tbl_25, 'tbl_26': tbl_26, 'tbl_27': tbl_27, 'tbl_28': tbl_28, 'tbl_29': tbl_29, 'tbl_30': tbl_30, 'tbl_31': tbl_31, 'tbl_32': tbl_32, 'tbl_33': tbl_33, 'tbl_34': tbl_34, 'tbl_35': tbl_35, 'tbl_36': tbl_36, 'tbl_37': tbl_37, 'tbl_38': tbl_38, 'tbl_39': tbl_39, 'W_top1': W_top1, 'b_top1': b_top1, 'W_top2': W_top2, 'b_top2': b_top2, 'W_top3': W_top3, 'L0_rec_W0': _L0_rec_in['W0'], 'L0_rec_b0': _L0_rec_in['b0'], 'L0_rec_W1': _L0_rec_in['W1'], 'L0_rec_b1': _L0_rec_in['b1'], 'L0_rec_W2': _L0_rec_in['W2'], 'L0_rec_b2': _L0_rec_in['b2']}

def reference(dense_ctx, ids, tbl_0, tbl_1, tbl_2, tbl_3, tbl_4, tbl_5, tbl_6, tbl_7, tbl_8, tbl_9, tbl_10, tbl_11, tbl_12, tbl_13, tbl_14, tbl_15, tbl_16, tbl_17, tbl_18, tbl_19, tbl_20, tbl_21, tbl_22, tbl_23, tbl_24, tbl_25, tbl_26, tbl_27, tbl_28, tbl_29, tbl_30, tbl_31, tbl_32, tbl_33, tbl_34, tbl_35, tbl_36, tbl_37, tbl_38, tbl_39, W_top1, b_top1, W_top2, b_top2, W_top3, L0_rec_W0, L0_rec_b0, L0_rec_W1, L0_rec_b1, L0_rec_W2, L0_rec_b2):
    import jax
    import jax.numpy as jnp

    def _L0_rec_ref(inputs, W0, b0, W1, b1, W2, b2):
        import jax, jax.numpy as jnp
        import numpy as np
        LAYER_SIZES = [200, 200, 200]
        params = [(W0, b0), (W1, b1), (W2, b2)]
        B, F, D = inputs.shape
        h = inputs
        outs = []
        n_layers = len(params)
        for i, (W, bias) in enumerate(params):
            x = jnp.einsum('bhd,bmd->bhmd', h, inputs).reshape(B, -1, D)
            y = jax.nn.relu(jnp.einsum('oi,bid->bod', W, x) + bias[None, :, None])
            if i != n_layers - 1:
                h, direct = jnp.split(y, 2, axis=1)
            else:
                direct = y
            outs.append(direct)
        result = jnp.concatenate(outs, axis=1)
        return result.sum(-1)
    e = jnp.stack([tbl_0[ids[:, 0]], tbl_1[ids[:, 1]], tbl_2[ids[:, 2]], tbl_3[ids[:, 3]], tbl_4[ids[:, 4]], tbl_5[ids[:, 5]], tbl_6[ids[:, 6]], tbl_7[ids[:, 7]], tbl_8[ids[:, 8]], tbl_9[ids[:, 9]], tbl_10[ids[:, 10]], tbl_11[ids[:, 11]], tbl_12[ids[:, 12]], tbl_13[ids[:, 13]], tbl_14[ids[:, 14]], tbl_15[ids[:, 15]], tbl_16[ids[:, 16]], tbl_17[ids[:, 17]], tbl_18[ids[:, 18]], tbl_19[ids[:, 19]], tbl_20[ids[:, 20]], tbl_21[ids[:, 21]], tbl_22[ids[:, 22]], tbl_23[ids[:, 23]], tbl_24[ids[:, 24]], tbl_25[ids[:, 25]], tbl_26[ids[:, 26]], tbl_27[ids[:, 27]], tbl_28[ids[:, 28]], tbl_29[ids[:, 29]], tbl_30[ids[:, 30]], tbl_31[ids[:, 31]], tbl_32[ids[:, 32]], tbl_33[ids[:, 33]], tbl_34[ids[:, 34]], tbl_35[ids[:, 35]], tbl_36[ids[:, 36]], tbl_37[ids[:, 37]], tbl_38[ids[:, 38]], tbl_39[ids[:, 39]]], axis=1)
    z = _L0_rec_ref(e, L0_rec_W0, L0_rec_b0, L0_rec_W1, L0_rec_b1, L0_rec_W2, L0_rec_b2)
    z = z.reshape(z.shape[0], -1)
    h = jnp.concatenate([z, dense_ctx], axis=1)
    h = jnp.maximum(h @ W_top1 + b_top1, 0.0)
    h = jnp.maximum(h @ W_top2 + b_top2, 0.0)
    y = h @ W_top3
    return y

_drawn_inputs = setup_inputs


def setup_inputs(seed=0):
    import zlib

    import numpy as np

    out = dict(_drawn_inputs(seed))
    spreads = {'b_top1': (0.0, 2.0),
     'b_top2': (0.0, 2.0),
     'L0_rec_b0': (0.0, 0.279),
     'L0_rec_b1': (0.0, 0.589),
     'L0_rec_b2': (0.0, 0.8)}
    factors = {'tbl_0': 8.0,
     'tbl_1': 8.0,
     'tbl_2': 8.0,
     'tbl_3': 8.0,
     'tbl_4': 8.0,
     'tbl_5': 8.0,
     'tbl_6': 8.0,
     'tbl_7': 8.0,
     'tbl_8': 8.0,
     'tbl_9': 8.0,
     'tbl_10': 8.0,
     'tbl_11': 8.0,
     'tbl_12': 8.0,
     'tbl_13': 8.0,
     'tbl_14': 8.0,
     'tbl_15': 8.0,
     'tbl_16': 8.0,
     'tbl_17': 8.0,
     'tbl_18': 8.0,
     'tbl_19': 8.0,
     'tbl_20': 8.0,
     'tbl_21': 8.0,
     'tbl_22': 8.0,
     'tbl_23': 8.0,
     'tbl_24': 8.0,
     'tbl_25': 8.0,
     'tbl_26': 8.0,
     'tbl_27': 8.0,
     'tbl_28': 8.0,
     'tbl_29': 8.0,
     'tbl_30': 8.0,
     'tbl_31': 8.0,
     'tbl_32': 8.0,
     'tbl_33': 8.0,
     'tbl_34': 8.0,
     'tbl_35': 8.0,
     'tbl_36': 8.0,
     'tbl_37': 8.0,
     'tbl_38': 8.0,
     'tbl_39': 8.0,
     'L0_rec_W0': 8.0,
     'L0_rec_W1': 8.0,
     'L0_rec_W2': 6.429,
     'dense_ctx': 8.0}
    for name, (base, spread) in spreads.items():
        noise = np.random.default_rng([zlib.crc32(name.encode()), seed]).standard_normal(out[name].shape)
        drawn = base * np.exp(spread * noise) if base else spread * noise
        out[name] = jnp.asarray(drawn.astype(out[name].dtype))
    for name, factor in factors.items():
        out[name] = (out[name] * factor).astype(out[name].dtype)
    return out
```

```python
from contextlib import ExitStack

import numpy as np
import concourse.bass as bass
from concourse import mybir

F32 = mybir.dt.float32
F32R = mybir.dt.float32r
I32 = mybir.dt.int32
ALU = mybir.AluOpType
ACT = mybir.ActivationFunctionType

P = 128
BATCH, FIELDS, DIM, DENSE = 512, 40, 32, 16
BLOCK_B = 16
COLS = BLOCK_B * DIM
BLOCKS = BATCH // BLOCK_B
HALF = 100
MAPS = 2 * HALF

DIST = 3
K0 = DIST * FIELDS
TILES0 = 7
K0_LAST = 2 * FIELDS + FIELDS // 2
PAIRS0 = (TILES0 + 1) // 2
WRAP = FIELDS // 2
ROWS_E = FIELDS + WRAP

GH, GM = 25, 5
K1 = GH * GM
HG, MG = HALF // GH, FIELDS // GM
TILES1 = HG * MG
PAIRS1 = TILES1 // 2
MP = MG // 2

PAIRS = PAIRS0 + 2 * PAIRS1
LEAD = PAIRS0 + PAIRS1
XBUF = 3
SBUFS = 3
assert PAIRS % XBUF == 0 and PAIRS % SBUFS == 0

GF = P // BLOCK_B
GATHERS = FIELDS // GF
WRITES = GATHERS + (WRAP + GF - 1) // GF

CHUNK = 4
CHUNKS = TILES1 // CHUNK
PREP = [(1, 0), (1, 1)]
for _k in range(CHUNKS):
    if _k + 2 < CHUNKS:
        PREP.append((1, _k + 2))
    PREP.append((2, _k))

H1T, H2T = 4, 2


def build_tower(nc, ids, base, table, w0a, w0b, w1, w2, bias, wt1, bt1, wt2, bt2, wt3, dense, out, scratch):
    with ExitStack() as ctx:
        def sb(name, shape, dt=F32):
            return ctx.enter_context(nc.sbuf_tensor(name, shape, dt))

        def sem(name):
            return ctx.enter_context(nc.semaphore(name))

        wh = [sb("wh0", [P, TILES0, MAPS], F32R), sb("wh1", [P, TILES1, MAPS], F32R), sb("wh2", [P, TILES1, MAPS], F32R)]
        wl = [sb("wl0", [P, TILES0, MAPS], F32R), sb("wl1", [P, TILES1, MAPS], F32R), sb("wl2", [P, TILES1, MAPS], F32R)]
        x = sb("x", [P, XBUF, 2, COLS])
        xh = sb("xh", [P, SBUFS, 2, COLS], F32R)
        xl = sb("xl", [P, SBUFS, 2, COLS], F32R)
        e_rep = sb("e_rep", [P, MG, COLS])
        e_near = sb("e_near", [P, 1, COLS])
        e_far = sb("e_far", [P, TILES0, COLS])
        h_rep = [sb("h_rep1", [P, HG, COLS]), sb("h_rep2", [P, HG, COLS])]
        h = sb("h", [HALF, COLS])
        z = sb("z", [HALF, 4, BATCH])
        bias_sb = sb("bias_sb", [HALF, 6])
        ids_sb = sb("ids_sb", [P, BLOCKS * GATHERS], I32)
        base_sb = sb("base_sb", [P, GATHERS], I32)
        idx = sb("idx", [P, GATHERS], I32)
        rows = sb("rows", [P, GATHERS, DIM])
        bt1_sb = sb("bt1_sb", [P, H1T])
        bt2_sb = sb("bt2_sb", [P, H2T])
        wt3_sb = sb("wt3_sb", [P, H2T])
        ps = ctx.enter_context(nc.psum_tensor("ps", [P, 8, COLS], F32))

        w0a_st = h_rep[0][:, :, :].rearrange("p a n -> p (a n)")[:, 0:TILES0 * MAPS].rearrange("p (t o) -> p t o", o=MAPS)
        w0b_st = h_rep[1][:, :, :].rearrange("p a n -> p (a n)")[:, 0:TILES0 * MAPS].rearrange("p (t o) -> p t o", o=MAPS)
        w_st = [h_rep[1][:, 2 * b:2 * b + 2, :].rearrange("p a n -> p (a n)")[:, 0:CHUNK * MAPS]
                .rearrange("p (t o) -> p t o", o=MAPS) for b in range(2)]
        far = e_far[:, :, :].rearrange("p t n -> p (t n)")
        wt1_sb = far[0:HALF, 0:2048].rearrange("p (c n) -> p c n", c=4)
        wt1d_sb = far[0:DENSE, 2048:2560]
        wt2_sb = far[:, 2560:3584].rearrange("p (k n) -> p k n", k=H1T)
        dense_sb = e_near[0:DENSE, 0, :]
        y_sb = e_rep[0:1, 0, :]
        g1 = h_rep[0]
        g2 = h_rep[1]

        ids_loaded = sem("ids_loaded")
        idx_ready = sem("idx_ready")
        gathered = sem("gathered")
        scratch_written = sem("scratch_written")
        w0_loaded = sem("w0_loaded")
        w0_summed = sem("w0_summed")
        w_loaded = [sem("w_loaded0"), sem("w_loaded1")]
        w_high = sem("w_high")
        w_low = sem("w_low")
        bias_loaded = sem("bias_loaded")
        e0_loaded = sem("e0_loaded")
        e_loaded = [sem(f"e_loaded{p}") for p in range(MP)]
        h_made = [sem("h_made1"), sem("h_made2")]
        h_loaded = [[sem(f"h_loaded{l}_{g}") for g in range(HG)] for l in (1, 2)]
        x_ready = sem("x_ready")
        xh_ready = sem("xh_ready")
        xl_ready = sem("xl_ready")
        x_used = sem("x_used")
        y_read = sem("y_read")
        top_loaded = sem("top_loaded")
        g1_sum = sem("g1_sum")
        g1_ready = sem("g1_ready")
        g2_sum = sem("g2_sum")
        g2_ready = sem("g2_ready")
        out_sum = sem("out_sum")
        out_ready = sem("out_ready")
        out_written = sem("out_written")

        def stage_tiles(layer, q):
            if layer == 0:
                return 2 * q, min(2, TILES0 - 2 * q), (K0 if 2 * q + 1 < TILES0 else K0_LAST)
            return 2 * q, 2, K1

        block = ctx.enter_context(nc.Block())

        @block.gpsimd
        def _(pool):
            pool.dma_start(ids_sb[:, :], ids).then_inc(ids_loaded, 16)
            pool.dma_start(base_sb[:, :], base).then_inc(ids_loaded, 16)
            pool.wait_ge(ids_loaded, 32)

            target = pool.alloc_register("target")

            def gather(b):
                nc.gpsimd.tensor_tensor(idx[:, :], ids_sb[:, bass.ds(b * GATHERS, GATHERS)], base_sb[:, :],
                                        ALU.add).then_inc(idx_ready, 1)
                pool.reg_mov(target, b + 1)
                pool.wait_ge(ids_loaded, 32)
                pool.wait_ge(idx_ready, target)
                for c in range(GATHERS):
                    pool.indirect_dma_start(rows[:, c, :], None, table,
                                            bass.IndirectOffsetOnAxis(ap=idx[:, c:c + 1], axis=0)).then_inc(gathered, 16)
                pool.wait_ge(gathered, (b + 1) * (16 * GATHERS))
                for c in range(GATHERS):
                    for f0, top in ((c * GF, FIELDS), (FIELDS + c * GF, ROWS_E)):
                        n = min(GF, top - f0)
                        if n > 0:
                            pool.dma_start(scratch[bass.ds(b * ROWS_E + f0, n), :].rearrange("f (s d) -> (f s) d", d=DIM),
                                           rows[0:n * BLOCK_B, c, :]).then_inc(scratch_written, 16)
                pool.wait_ge(scratch_written, (b + 1) * (16 * WRITES))

            gather(0)
            with pool.Fori(1, BLOCKS) as b:
                gather(b)

        @block.sync
        def _(sp):
            target = sp.alloc_register("target")

            def after(signal, count):
                if not isinstance(count, int):
                    sp.reg_mov(target, count)
                    count = target
                sp.wait_ge(bias_loaded, 16)
                sp.wait_ge(signal, count)

            def load_e0(b):
                after(scratch_written, (b + 1) * (16 * WRITES))
                sp.dma_start(e_near[0:K0, 0, :], scratch[bass.ds(b * ROWS_E, FIELDS), :].unsqueeze(0)
                             .broadcast_to([DIST, FIELDS, COLS])).then_inc(e0_loaded, 16)
                for kk in range(DIST):
                    first = scratch[bass.ds(b * ROWS_E + kk, FIELDS), :]
                    sp.dma_start(e_far[kk * FIELDS:(kk + 1) * FIELDS, :, :],
                                 bass.AP(first.tensor, first.offset, [[COLS, FIELDS], [DIST * COLS, TILES0], [1, COLS]]))\
                      .then_inc(e0_loaded, 16)

            def load_e(b, p):
                for a in range(2):
                    j = 2 * p + a
                    sp.dma_start(e_rep[0:K1, j, :], scratch[bass.ds(b * ROWS_E + GM * j, GM), :].unsqueeze(0)
                                 .broadcast_to([GH, GM, COLS])).then_inc(e_loaded[p], 16)

            def load_h(layer, count):
                after(h_made[layer - 1], count)
                for g in range(HG):
                    sp.dma_start(h_rep[layer - 1][0:K1, g, :],
                                 h[GH * g:GH * (g + 1), :].unsqueeze(1)
                                 .broadcast_to([GH, GM, COLS])).then_inc(h_loaded[layer - 1][g], 16)

            sp.dma_start(w0a_st, w0a).then_inc(w0_loaded, 16)
            sp.dma_start(w0b_st, w0b).then_inc(w0_loaded, 16)
            sp.dma_start(bias_sb[:, :], bias).then_inc(bias_loaded, 16)
            load_e0(0)
            for p in range(MP):
                load_e(0, p)

            def load_w(n):
                layer, c = PREP[n]
                if n < 2:
                    sp.wait_ge(w0_summed, 1)
                else:
                    sp.wait_ge(w_low, n)
                sp.dma_start(w_st[n % 2], (w1, w2)[layer - 1][:, c * CHUNK:(c + 1) * CHUNK, :]).then_inc(w_loaded[n % 2], 16)

            load_w(0)
            load_w(1)
            load_h(1, 1)
            for n in range(2, len(PREP)):
                load_w(n)
            sp.wait_ge(x_ready, PAIRS0)
            load_e0(1)
            sp.wait_ge(w_low, 1 + len(PREP))

            def turn(i, last):
                at = i * PAIRS + LEAD
                after(x_ready, i * PAIRS + PAIRS0)
                load_h(2, i + 1)
                after(x_ready, at + PAIRS0)
                load_h(1, i + 2)
                if not last:
                    load_e0(i + 2)
                for p in range(MP):
                    after(x_ready, at + (PAIRS0 + HG * (p + 1)))
                    load_e(i + 1, p)

            with sp.Fori(0, BLOCKS - 2) as i:
                turn(i, False)
            turn(BLOCKS - 2, True)
            sp.wait_ge(x_ready, PAIRS * (BLOCKS - 1) + PAIRS0)
            load_h(2, BLOCKS)
            sp.dma_start(wt1_sb, wt1[0:4 * HALF, :].rearrange("(c p) n -> p c n", c=4)).then_inc(top_loaded, 16)
            sp.dma_start(wt1d_sb, wt1[4 * HALF:, :]).then_inc(top_loaded, 16)
            sp.dma_start(wt2_sb, wt2.rearrange("(k p) n -> p k n", k=H1T)).then_inc(top_loaded, 16)
            sp.dma_start(dense_sb, dense).then_inc(top_loaded, 16)
            sp.dma_start(bt1_sb[:, :], bt1).then_inc(top_loaded, 16)
            sp.dma_start(bt2_sb[:, :], bt2).then_inc(top_loaded, 16)
            sp.dma_start(wt3_sb[:, :], wt3).then_inc(top_loaded, 16)
            sp.wait_ge(out_ready, 1)
            sp.dma_start(out, y_sb).then_inc(out_written, 16)
            sp.wait_ge(out_written, 16)

        @block.vector
        def _(dve):
            def multiply(layer, q, turn, s, b):
                t, tiles, k = stage_tiles(layer, q)
                n = turn * PAIRS + s
                if not isinstance(n, int) or n >= XBUF:
                    dve.wait_ge(xl_ready, n - (XBUF - 1))
                o = x[0:k, s % XBUF, 0:tiles, :]
                if layer == 0:
                    if q == 0:
                        dve.wait_ge(e0_loaded, (b + 1) * (16 * (1 + DIST)))
                    near = e_near[0:k, 0:1, :].broadcast_to([k, tiles, COLS])
                    far_ = e_far[0:k, t:t + tiles, :]
                    nc.vector.tensor_tensor(o, near, far_, ALU.mult).then_inc(x_ready, 1)
                    return
                p, g = q // HG, q % HG
                if p == 0:
                    dve.wait_ge(h_loaded[layer - 1][g], (b + 1) * 16)
                if g == 0 and layer == 1:
                    dve.wait_ge(e_loaded[p], (b + 1) * 32)
                nc.vector.tensor_tensor(o, h_rep[layer - 1][0:k, g:g + 1, :].broadcast_to([k, tiles, COLS]),
                                        e_rep[0:k, 2 * p:2 * p + 2, :], ALU.mult).then_inc(x_ready, 1)

            def low_part(layer, q, turn, s):
                t, tiles, k = stage_tiles(layer, q)
                n = turn * PAIRS + s
                dve.wait_ge(xh_ready, n + 1)
                if not isinstance(n, int) or n >= SBUFS:
                    dve.wait_ge(x_used, n - (SBUFS - 1))
                nc.vector.tensor_tensor(xl[0:k, s % SBUFS, 0:tiles, :], x[0:k, s % XBUF, 0:tiles, :],
                                        xh[0:k, s % SBUFS, 0:tiles, :].bitcast(F32), ALU.subtract).then_inc(xl_ready, 1)

            def w_low_part(n):
                if n == 0:
                    src, layer, t, tiles, k = w0a_st, 0, 0, TILES0, K0
                else:
                    layer, c = PREP[n - 1]
                    src, t, tiles, k = w_st[(n - 1) % 2], c * CHUNK, CHUNK, K1
                dve.wait_ge(w_high, n + 1)
                nc.vector.tensor_tensor(wl[layer][0:k, t:t + tiles, :], src[0:k],
                                        wh[layer][0:k, t:t + tiles, :].bitcast(F32), ALU.subtract).then_inc(w_low, 1)

            dve.wait_ge(w0_loaded, 32)
            nc.vector.tensor_tensor(w0a_st[0:K0], w0a_st[0:K0], w0b_st[0:K0], ALU.add).then_inc(w0_summed, 1)
            w_low_part(0)
            for q in range(PAIRS0):
                multiply(0, q, 0, q, 0)
                if q:
                    low_part(0, q - 1, 0, q - 1)
            low_part(0, PAIRS0 - 1, 0, PAIRS0 - 1)
            w_low_part(1)
            w_low_part(2)
            prepared = 3
            for q in range(PAIRS1):
                multiply(1, q, 0, PAIRS0 + q, 0)
                if q:
                    low_part(1, q - 1, 0, PAIRS0 + q - 1)
                if q % 2:
                    while prepared < min(3 + q + 1, 1 + len(PREP)):
                        w_low_part(prepared)
                        prepared += 1
            assert prepared == 1 + len(PREP)

            ORDER = [(0, q, 1) for q in range(PAIRS0)] + [(2, q, 0) for q in range(PAIRS1)] + [(1, q, 1) for q in range(PAIRS1)]
            with dve.Fori(0, BLOCKS - 1) as i:
                for s, (layer, q, ahead) in enumerate(ORDER):
                    multiply(layer, q, i, LEAD + s, i + ahead)
                    before = ORDER[s - 1]
                    low_part(before[0], before[1], i, LEAD + s - 1)
            low_part(1, PAIRS1 - 1, BLOCKS - 1, LEAD - 1)
            for q in range(PAIRS1):
                multiply(2, q, BLOCKS - 1, LEAD + q, BLOCKS - 1)
                if q:
                    low_part(2, q - 1, BLOCKS - 1, LEAD + q - 1)
            low_part(2, PAIRS1 - 1, BLOCKS - 1, LEAD + PAIRS1 - 1)
            dve.wait_ge(out_sum, 1)
            nc.vector.tensor_copy(y_sb, ps[0:1, 6, :]).then_inc(out_ready, 1)

        @block.scalar
        def _(act):
            def high_part(layer, q, turn, s):
                t, tiles, k = stage_tiles(layer, q)
                n = turn * PAIRS + s
                act.wait_ge(x_ready, n + 1)
                if not isinstance(n, int) or n >= SBUFS:
                    act.wait_ge(x_used, n - (SBUFS - 1))
                nc.scalar.activation(xh[0:k, s % SBUFS, 0:tiles, :], x[0:k, s % XBUF, 0:tiles, :],
                                     ACT.Copy).then_inc(xh_ready, 1)

            def w_high_part(n):
                if n == 0:
                    src, layer, t, tiles, k = w0a_st, 0, 0, TILES0, K0
                    act.wait_ge(w0_summed, 1)
                else:
                    layer, c = PREP[n - 1]
                    src, t, tiles, k = w_st[(n - 1) % 2], c * CHUNK, CHUNK, K1
                    act.wait_ge(w_loaded[(n - 1) % 2], 16 * ((n - 1) // 2 + 1))
                nc.scalar.activation(wh[layer][0:k, t:t + tiles, :], src[0:k], ACT.Copy).then_inc(w_high, 1)

            def hidden(layer, pairs):
                act.wait_ge(x_used, pairs)
                nc.scalar.activation(h[:, :], ps[0:HALF, 2 * layer, :], ACT.Relu,
                                     bias=bias_sb[:, 2 * layer:2 * layer + 1]).then_inc(h_made[layer], 1)

            def direct(layer, part, b, s, last=False):
                y = ps[0:HALF, 2 * layer + part, s * DIM:(s + 1) * DIM]
                c = layer if layer < 2 else 2 + part
                ins = nc.scalar.activation(y, y, ACT.Relu, bias=bias_sb[:, 2 * layer + part:2 * layer + part + 1],
                                           accum_out=z[:, c, bass.ds(b * BLOCK_B + s, 1)])
                if last:
                    ins.then_inc(y_read, 1)

            def directs(layer, parts, b):
                jobs = [(layer, part, b, s) for part in parts for s in range(BLOCK_B)]
                return [(*j, n == len(jobs) - 1) for n, j in enumerate(jobs)]

            w_high_part(0)
            act.wait_ge(bias_loaded, 16)
            for q in range(PAIRS0):
                high_part(0, q, 0, q)
            w_high_part(1)
            w_high_part(2)
            hidden(0, PAIRS0)
            todo = directs(0, [1], 0)
            prepared = 3
            for q in range(PAIRS1):
                high_part(1, q, 0, PAIRS0 + q)
                if q % 2:
                    while prepared < min(3 + q + 1, 1 + len(PREP)):
                        w_high_part(prepared)
                        prepared += 1
                direct(*todo.pop(0))

            def turn(i):
                ORDER = [(0, q) for q in range(PAIRS0)] + [(2, q) for q in range(PAIRS1)] + [(1, q) for q in range(PAIRS1)]
                todo = []
                for s, (layer, q) in enumerate(ORDER):
                    high_part(layer, q, i, LEAD + s)
                    if s == SBUFS - 1:
                        hidden(1, i * PAIRS + LEAD)
                        todo += directs(1, [1], i)
                    elif s == PAIRS0 + HG - 1:
                        hidden(0, i * PAIRS + (LEAD + PAIRS0))
                        todo += directs(0, [1], i + 1)
                    elif s == PAIRS0 + PAIRS1 + SBUFS - 1:
                        act.wait_ge(x_used, i * PAIRS + (LEAD + PAIRS0 + PAIRS1))
                        todo += directs(2, [0, 1], i)
                    else:
                        for _ in range(3):
                            if todo:
                                direct(*todo.pop(0))
                while todo:
                    direct(*todo.pop(0))

            with act.Fori(0, BLOCKS - 1) as i:
                turn(i)
            hidden(1, PAIRS * (BLOCKS - 1) + LEAD)
            todo = directs(1, [1], BLOCKS - 1)
            for q in range(PAIRS1):
                high_part(2, q, BLOCKS - 1, LEAD + q)
                if q >= 2 and todo:
                    for _ in range(2):
                        if todo:
                            direct(*todo.pop(0))
            act.wait_ge(x_used, PAIRS * BLOCKS)
            for job in directs(2, [0, 1], BLOCKS - 1):
                direct(*job)
            act.wait_ge(top_loaded, 16 * 7)
            for m in range(H1T):
                act.wait_ge(g1_sum, m + 1)
                nc.scalar.activation(g1[:, m, :], ps[:, m, :], ACT.Relu, bias=bt1_sb[:, m:m + 1]).then_inc(g1_ready, 1)
            for m in range(H2T):
                act.wait_ge(g2_sum, m + 1)
                nc.scalar.activation(g2[:, m, :], ps[:, 4 + m, :], ACT.Relu, bias=bt2_sb[:, m:m + 1]).then_inc(g2_ready, 1)

        @block.tensor
        def _(pe):
            def contract(layer, q, turn, at):
                n, s = turn * PAIRS + at, at % SBUFS
                t0, tiles, k_ = stage_tiles(layer, q)
                total = TILES0 if layer == 0 else TILES1

                def mm(half, w, xs, a, start, stop):
                    t = t0 + a
                    return nc.tensor.matmul(ps[0:HALF, 2 * layer + half, :], w[layer][0:k_, t, half * HALF:(half + 1) * HALF],
                                            xs[0:k_, s, a, :], start=start, stop=stop)

                pe.wait_ge(xh_ready, n + 1)
                for a in range(tiles):
                    for half in range(2):
                        mm(half, wh, xh, a, t0 + a == 0, False)
                        mm(half, wl, xh, a, False, False)
                pe.wait_ge(xl_ready, n + 1)
                for a in range(tiles):
                    for half in range(2):
                        last = mm(half, wh, xl, a, False, t0 + a == total - 1)
                last.then_inc(x_used, 1)

            pe.wait_ge(w_low, 1)
            for q in range(PAIRS0):
                contract(0, q, 0, q)
            for q in range(PAIRS1):
                if q % 2 == 0:
                    pe.wait_ge(w_low, 2 + PREP.index((1, q // 2)))
                contract(1, q, 0, PAIRS0 + q)
            pe.wait_ge(w_low, 1 + len(PREP))
            with pe.Fori(0, BLOCKS - 1) as i:
                pe.wait_ge(y_read, i * 3 + 1)
                for q in range(PAIRS0):
                    contract(0, q, i, LEAD + q)
                for q in range(PAIRS1):
                    contract(2, q, i, LEAD + PAIRS0 + q)
                pe.wait_ge(y_read, i * 3 + 2)
                for q in range(PAIRS1):
                    contract(1, q, i, LEAD + PAIRS0 + PAIRS1 + q)
            pe.wait_ge(y_read, 3 * (BLOCKS - 1) + 1)
            for q in range(PAIRS1):
                contract(2, q, BLOCKS - 1, LEAD + q)
            pe.wait_ge(top_loaded, 16 * 7)
            pe.wait_ge(y_read, 3 * BLOCKS)
            for m in range(H1T):
                for c in range(4):
                    nc.tensor.matmul(ps[:, m, :], wt1_sb[:, c, m * P:(m + 1) * P], z[:, c, :], start=(c == 0), stop=False)
                nc.tensor.matmul(ps[:, m, :], wt1d_sb[:, m * P:(m + 1) * P], dense_sb, start=False, stop=True).then_inc(g1_sum, 1)
            for k in range(H1T):
                pe.wait_ge(g1_ready, k + 1)
                for m in range(H2T):
                    last = nc.tensor.matmul(ps[:, 4 + m, :], wt2_sb[:, k, m * P:(m + 1) * P], g1[:, k, :],
                                            start=(k == 0), stop=(k == H1T - 1))
                    if k == H1T - 1:
                        last.then_inc(g2_sum, 1)
            for k in range(H2T):
                pe.wait_ge(g2_ready, k + 1)
                last = nc.tensor.matmul(ps[0:1, 6, :], wt3_sb[:, k:k + 1], g2[:, k, :], start=(k == 0), stop=(k == H2T - 1))
            last.then_inc(out_sum, 1)


def kernel(**inputs):
    import concourse.bacc as bacc
    from concourse.bass_utils import run_bass_kernel_spmd

    tables = [np.asarray(inputs[f"tbl_{f}"]) for f in range(FIELDS)]
    starts = np.concatenate([[0], np.cumsum([t.shape[0] for t in tables])[:-1]]).astype(np.int32)

    def lane(a, rows=P):
        return np.concatenate([a, np.zeros((rows - a.shape[0], *a.shape[1:]), a.dtype)]) if a.shape[0] < rows else a

    def cin_weights(w):
        w = np.asarray(w).reshape(MAPS, HG, GH, MP, 2, GM)
        return lane(np.ascontiguousarray(w.transpose(2, 5, 3, 1, 4, 0)).reshape(K1, TILES1, MAPS))

    w0 = np.asarray(inputs["L0_rec_W0"]).reshape(MAPS, FIELDS, FIELDS)
    near = np.zeros((DIST, FIELDS, TILES0, MAPS), w0.dtype)
    far = np.zeros((DIST, FIELDS, TILES0, MAPS), w0.dtype)
    for k in range(FIELDS // 2 + 1):
        for hh in range(FIELDS if k < FIELDS // 2 else FIELDS // 2):
            m = (hh + k) % FIELDS
            near[k % DIST, hh, k // DIST] = w0[:, hh, m]
            if k:
                far[k % DIST, hh, k // DIST] = w0[:, m, hh]

    def cols(v, n):
        return np.ascontiguousarray(np.asarray(v).reshape(n, -1).T)

    arrays = {
        "ids": np.ascontiguousarray(np.asarray(inputs["ids"]).reshape(BLOCKS, BLOCK_B, GATHERS, GF).transpose(3, 1, 0, 2)
                                    .reshape(P, BLOCKS * GATHERS)),
        "base": np.ascontiguousarray(np.repeat(starts.reshape(GATHERS, GF).T, BLOCK_B, axis=0)),
        "table": np.concatenate(tables),
        "w0a": lane(near.reshape(K0, TILES0, MAPS)),
        "w0b": lane(far.reshape(K0, TILES0, MAPS)),
        "w1": cin_weights(inputs["L0_rec_W1"]),
        "w2": cin_weights(inputs["L0_rec_W2"]),
        "bias": np.concatenate([cols(inputs[f"L0_rec_b{n}"], 2) for n in range(3)], axis=1),
        "wt1": np.asarray(inputs["W_top1"]),
        "bt1": cols(inputs["b_top1"], H1T),
        "wt2": np.asarray(inputs["W_top2"]),
        "bt2": cols(inputs["b_top2"], H2T),
        "wt3": cols(inputs["W_top3"], H2T),
        "dense": np.ascontiguousarray(np.asarray(inputs["dense_ctx"]).T),
    }
    nc = bacc.Bacc("TRN2", target_bir_lowering=False, num_devices=1)
    args = {k: nc.dram_tensor(f"in_{k}", a.shape, mybir.dt.from_np(a.dtype), kind="ExternalInput").ap()
            for k, a in arrays.items()}
    args["out"] = nc.dram_tensor("out_y", (1, BATCH), F32, kind="ExternalOutput").ap()
    args["scratch"] = nc.dram_tensor("scratch_e", (BLOCKS * ROWS_E, COLS), F32, kind="Internal").ap()
    build_tower(nc, **args)
    r = run_bass_kernel_spmd(nc, [{f"in_{k}": a for k, a in arrays.items()}], core_ids=[0])
    return r.results[0]["out_y"].reshape(BATCH, 1)
```

```python
from contextlib import ExitStack

import numpy as np
import concourse.bass as bass
from concourse import mybir

F32 = mybir.dt.float32
F32R = mybir.dt.float32r
I32 = mybir.dt.int32
ALU = mybir.AluOpType
ACT = mybir.ActivationFunctionType

P = 128
BATCH, FIELDS, DIM, DENSE = 512, 40, 32, 16
BLOCK_B = 16
COLS = BLOCK_B * DIM
BLOCKS = BATCH // BLOCK_B
HALF = 100
MAPS = 2 * HALF

DIST = 3
K0 = DIST * FIELDS
TILES0 = 7
K0_LAST = 2 * FIELDS + FIELDS // 2
PAIRS0 = (TILES0 + 1) // 2
WRAP = FIELDS // 2
ROWS_E = FIELDS + WRAP

GH, GM = 25, 5
K1 = GH * GM
HG, MG = HALF // GH, FIELDS // GM
SPREAD = [(0, 16), (16, GH - 16)]
TILES1 = HG * MG
PAIRS1 = TILES1 // 2
MP = MG // 2

PAIRS = PAIRS0 + 2 * PAIRS1
LEAD = PAIRS0 + PAIRS1
XBUF = 3
SBUFS = 3
assert PAIRS % XBUF == 0 and PAIRS % SBUFS == 0

GF = P // BLOCK_B
GATHERS = FIELDS // GF
WRITES = GATHERS + (WRAP + GF - 1) // GF

CHUNK = 4
CHUNKS = TILES1 // CHUNK
AHEAD = 6
PREP = [(1, _c) for _c in range(CHUNKS)] + [(2, _c) for _c in range(CHUNKS)]
STAGED = 3

ZC = 4
ZROWS = HALF + DENSE // ZC
EARLY = BATCH - BLOCK_B
H1T, H2T = 4, 2
TOP_LOADS = 6


def g1_bank(m):
    return (6, 7, 0, 1)[m]


def g2_bank(m):
    return (6, 7)[m]


OUT_BANK = 0


def build_tower(nc, ids, base, table, w0a, w0b, w1, w2, bias, wt1, bt1, wt2, bt2, wt3, dense, out, scratch):
    with ExitStack() as ctx:
        def sb(name, shape, dt=F32):
            return ctx.enter_context(nc.sbuf_tensor(name, shape, dt))

        def sem(name):
            return ctx.enter_context(nc.semaphore(name))

        wh = [sb("wh0", [P, TILES0, MAPS], F32R), sb("wh1", [P, TILES1, MAPS], F32R), sb("wh2", [P, TILES1, MAPS], F32R)]
        wl = [sb("wl0", [P, TILES0, MAPS], F32R), sb("wl1", [P, TILES1, MAPS], F32R), sb("wl2", [P, TILES1, MAPS], F32R)]
        x = sb("x", [P, XBUF, 2, COLS])
        xh = sb("xh", [P, SBUFS, 2, COLS], F32R)
        xl = sb("xl", [P, SBUFS, 2, COLS], F32R)
        e_rep = sb("e_rep", [P, MG, COLS])
        e_near = sb("e_near", [P, 1, COLS])
        e_far = sb("e_far", [P, TILES0, COLS])
        h_rep = [sb("h_rep1", [P, HG, COLS]), sb("h_rep2", [P, HG, COLS])]
        h = sb("h", [P, COLS])
        z = sb("z", [P, 4, BATCH])
        bias_sb = sb("bias_sb", [HALF, 6])
        ids_sb = sb("ids_sb", [P, BLOCKS * GATHERS], I32)
        base_sb = sb("base_sb", [P, GATHERS], I32)
        idx = sb("idx", [P, GATHERS], I32)
        rows = sb("rows", [P, GATHERS, DIM])
        bt1_sb = sb("bt1_sb", [P, H1T])
        bt2_sb = sb("bt2_sb", [P, H2T])
        wt3_sb = sb("wt3_sb", [P, H2T])
        ps = ctx.enter_context(nc.psum_tensor("ps", [P, 8, COLS], F32))

        w0a_st = h_rep[0][:, :, :].rearrange("p a n -> p (a n)")[:, 0:TILES0 * MAPS].rearrange("p (t o) -> p t o", o=MAPS)
        w0b_st = h_rep[1][:, :, :].rearrange("p a n -> p (a n)")[:, 0:TILES0 * MAPS].rearrange("p (t o) -> p t o", o=MAPS)
        w_st = [room.rearrange("p a n -> p (a n)")[:, 0:CHUNK * MAPS].rearrange("p (t o) -> p t o", o=MAPS)
                for room in (h_rep[1][:, 0:2, :], h_rep[1][:, 2:4, :], z[:, 2:4, :],
                             e_rep[:, 2:4, :], e_rep[:, 4:6, :], e_rep[:, 6:8, :])]
        far = e_far[:, :, :].rearrange("p t n -> p (t n)")
        wt1_sb = far[0:ZROWS, 0:2048].rearrange("p (c n) -> p c n", c=ZC)
        wt2_sb = far[:, 2048:3072].rearrange("p (k n) -> p k n", k=H1T)
        g1 = [h_rep[0][:, m, :] for m in range(H1T)]
        g2 = [far[:, 3072:3584], e_near[:, 0, :]]
        y_sb = h[0:1, :]

        ids_loaded = sem("ids_loaded")
        idx_ready = sem("idx_ready")
        gathered = sem("gathered")
        gathered0 = [sem(f"gathered0_{c}") for c in range(GATHERS)]
        scratch_written = sem("scratch_written")
        scratch0_written = sem("scratch0_written")
        w0_loaded = sem("w0_loaded")
        w0_summed = sem("w0_summed")
        w_loaded = [sem(f"w_loaded{b}") for b in range(AHEAD)]
        w_high = sem("w_high")
        w_low = sem("w_low")
        w2_low = sem("w2_low")
        bias_loaded = sem("bias_loaded")
        e0_loaded = [sem(f"e0_loaded{q}") for q in range(PAIRS0)]
        e_loaded = [sem(f"e_loaded{p}") for p in range(MP)]
        h_made = [sem("h_made1"), sem("h_made2")]
        h_loaded = [[sem(f"h_loaded{l}_{g}") for g in range(HG)] for l in (1, 2)]
        x_ready = sem("x_ready")
        xh_ready = sem("xh_ready")
        xl_ready = sem("xl_ready")
        x_used = sem("x_used")
        y_read = sem("y_read")
        top_loaded = sem("top_loaded")
        g1_sum = sem("g1_sum")
        g1_ready = sem("g1_ready")
        g2_sum = sem("g2_sum")
        g2_ready = sem("g2_ready")
        out_sum = sem("out_sum")
        y2_last = sem("y2_last")
        z_last = sem("z_last")
        out_ready = sem("out_ready")
        out_written = sem("out_written")

        def stage_tiles(layer, q):
            if layer == 0:
                return 2 * q, min(2, TILES0 - 2 * q), (K0 if 2 * q + 1 < TILES0 else K0_LAST)
            return 2 * q, 2, K1

        block = ctx.enter_context(nc.Block())

        def w_room(n):
            return (n, 1) if n < AHEAD else (n % STAGED, n // STAGED)

        def w_split(layer, c):
            return (w_low, 2 + c) if layer == 1 else (w2_low, 1 + c)

        def write_rows(eng, b, c, f0, top, written):
            n = min(GF, top - f0)
            eng.dma_start(scratch[bass.ds(b * ROWS_E + f0, n), :].rearrange("f (s d) -> (f s) d", d=DIM),
                          rows[0:n * BLOCK_B, c, :]).then_inc(written, 16)

        @block.gpsimd
        def _(pool):
            pool.wait_ge(ids_loaded, 32)

            target = pool.alloc_register("target")

            def gather(b, first=False):
                nc.gpsimd.tensor_tensor(idx[:, :], ids_sb[:, bass.ds(b * GATHERS, GATHERS)], base_sb[:, :],
                                        ALU.add).then_inc(idx_ready, 1)
                pool.reg_mov(target, b + 1)
                pool.wait_ge(ids_loaded, 32)
                pool.wait_ge(idx_ready, target)
                for c in range(GATHERS):
                    landed = gathered0[c] if first else gathered
                    pool.indirect_dma_start(rows[:, c, :], None, table,
                                            bass.IndirectOffsetOnAxis(ap=idx[:, c:c + 1], axis=0)).then_inc(landed, 16)
                if not first:
                    pool.wait_ge(gathered, b * (16 * GATHERS))
                    for c in range(GATHERS):
                        write_rows(pool, b, c, GF * c, FIELDS, scratch_written)
                        if GF * c < WRAP:
                            write_rows(pool, b, c, FIELDS + GF * c, ROWS_E, scratch_written)
                if first:
                    pool.wait_ge(scratch0_written, 16 * WRITES)
                else:
                    pool.wait_ge(scratch_written, b * (16 * WRITES))

            gather(0, first=True)
            gather(1)
            for c in range(CHUNKS):
                n = PREP.index((2, c))
                pool.wait_ge(w_high, n + 2)
                nc.gpsimd.tensor_tensor(wl[2][0:K1, c * CHUNK:(c + 1) * CHUNK, :], w_st[w_room(n)[0]][0:K1],
                                        wh[2][0:K1, c * CHUNK:(c + 1) * CHUNK, :].bitcast(F32),
                                        ALU.subtract).then_inc(w2_low, 1)
            with pool.Fori(2, BLOCKS) as b:
                gather(b)

        @block.sync
        def _(sp):
            target = sp.alloc_register("target")

            def after(signal, count):
                if not isinstance(count, int):
                    sp.reg_mov(target, count)
                    count = target
                sp.wait_ge(bias_loaded, 16)
                sp.wait_ge(signal, count)

            def load_e0(b):
                if isinstance(b, int) and b == 0:
                    sp.wait_ge(scratch0_written, 16 * WRITES)
                else:
                    after(scratch_written, b * (16 * WRITES))
                sp.dma_start(e_near[0:K0, 0, :], scratch[bass.ds(b * ROWS_E, FIELDS), :].unsqueeze(0)
                             .broadcast_to([DIST, FIELDS, COLS])).then_inc(e0_loaded[0], 16)
                for t in range(TILES0):
                    first = scratch[bass.ds(b * ROWS_E + DIST * t, FIELDS), :]
                    sp.dma_start(e_far[0:K0, t, :], bass.AP(first.tensor, first.offset, [[COLS, DIST], [COLS, FIELDS], [1, COLS]]))\
                      .then_inc(e0_loaded[t // 2], 16)

            def load_e(b, p):
                for a in range(2):
                    j = 2 * p + a
                    sp.dma_start(e_rep[0:K1, j, :], scratch[bass.ds(b * ROWS_E + GM * j, GM), :].unsqueeze(0)
                                 .broadcast_to([GH, GM, COLS])).then_inc(e_loaded[p], 16)

            def load_h(layer, count):
                after(h_made[layer - 1], count)
                for g in range(HG):
                    for h0, hn in SPREAD:
                        sp.dma_start(h_rep[layer - 1][GM * h0:GM * (h0 + hn), g, :],
                                     h[GH * g + h0:GH * g + h0 + hn, :].unsqueeze(1)
                                     .broadcast_to([hn, GM, COLS])).then_inc(h_loaded[layer - 1][g], 16)

            sp.dma_start(ids_sb[:, :], ids).then_inc(ids_loaded, 16)
            sp.dma_start(base_sb[:, :], base).then_inc(ids_loaded, 16)
            sp.dma_start(w0a_st, w0a).then_inc(w0_loaded, 16)
            sp.dma_start(w0b_st, w0b).then_inc(w0_loaded, 16)
            sp.dma_start(bias_sb[:, :], bias).then_inc(bias_loaded, 16)
            for c in range(GATHERS):
                sp.wait_ge(gathered0[c], 16)
                write_rows(sp, 0, c, GF * c, FIELDS, scratch0_written)
            load_e0(0)

            def load_w(n):
                layer, c = PREP[n]
                if n < 2:
                    sp.wait_ge(w0_summed, 1)
                elif n >= AHEAD:
                    before = n - AHEAD if n < AHEAD + STAGED else n - STAGED
                    sp.wait_ge(*w_split(*PREP[before]))
                sp.dma_start(w_st[w_room(n)[0]], (w1, w2)[layer - 1][:, c * CHUNK:(c + 1) * CHUNK, :]).then_inc(w_loaded[w_room(n)[0]], 16)

            load_e(0, 0)
            for n in range(AHEAD):
                load_w(n)
            load_h(1, 1)
            for p in range(1, MP):
                sp.wait_ge(*w_split(1, AHEAD - MP + p))
                load_e(0, p)
            for n in range(AHEAD, len(PREP)):
                load_w(n)
            sp.wait_ge(x_ready, PAIRS0)
            load_e0(1)
            sp.wait_ge(*w_split(1, CHUNKS - 1))
            sp.wait_ge(*w_split(2, CHUNKS - 1))
            sp.dma_start(z[HALF:ZROWS, :, :], dense.rearrange("(p c) b -> p c b", c=ZC)).then_inc(top_loaded, 16)
            sp.dma_start(bt1_sb[:, :], bt1).then_inc(top_loaded, 16)
            sp.dma_start(bt2_sb[:, :], bt2).then_inc(top_loaded, 16)
            sp.dma_start(wt3_sb[:, :], wt3).then_inc(top_loaded, 16)

            def turn(i, last):
                at = i * PAIRS + LEAD
                after(x_ready, i * PAIRS + PAIRS0)
                load_h(2, i + 1)
                after(x_ready, at + PAIRS0)
                load_h(1, i + 2)
                if not last:
                    load_e0(i + 2)
                else:
                    sp.dma_start(wt1_sb, wt1).then_inc(top_loaded, 16)
                    sp.dma_start(wt2_sb, wt2.rearrange("(k p) n -> p k n", k=H1T)).then_inc(top_loaded, 16)
                for p in range(MP):
                    after(x_ready, at + (PAIRS0 + HG * (p + 1)))
                    load_e(i + 1, p)

            with sp.Fori(0, BLOCKS - 2) as i:
                turn(i, False)
            turn(BLOCKS - 2, True)
            sp.wait_ge(x_ready, PAIRS * (BLOCKS - 1) + PAIRS0)
            load_h(2, BLOCKS)
            sp.wait_ge(out_ready, 2)
            sp.dma_start(out, y_sb).then_inc(out_written, 16)
            sp.wait_ge(out_written, 16)

        @block.vector
        def _(dve):
            def multiply(layer, q, turn, s, b):
                t, tiles, k = stage_tiles(layer, q)
                n = turn * PAIRS + s
                if not isinstance(n, int) or n >= XBUF:
                    dve.wait_ge(xl_ready, n - (XBUF - 1))
                o = x[0:k, s % XBUF, 0:tiles, :]
                if layer == 0:
                    dve.wait_ge(e0_loaded[q], (b + 1) * (16 * (tiles + (1 if q == 0 else 0))))
                    near = e_near[0:k, 0:1, :].broadcast_to([k, tiles, COLS])
                    far_ = e_far[0:k, t:t + tiles, :]
                    nc.vector.tensor_tensor(o, near, far_, ALU.mult).then_inc(x_ready, 1)
                    return
                p, g = q // HG, q % HG
                if p == 0:
                    dve.wait_ge(h_loaded[layer - 1][g], (b + 1) * (16 * len(SPREAD)))
                if g == 0 and layer == 1:
                    dve.wait_ge(e_loaded[p], (b + 1) * (2 * 16))
                nc.vector.tensor_tensor(o, h_rep[layer - 1][0:k, g:g + 1, :].broadcast_to([k, tiles, COLS]),
                                        e_rep[0:k, 2 * p:2 * p + 2, :], ALU.mult).then_inc(x_ready, 1)

            def low_part(layer, q, turn, s):
                t, tiles, k = stage_tiles(layer, q)
                n = turn * PAIRS + s
                dve.wait_ge(xh_ready, n + 1)
                if not isinstance(n, int) or n >= SBUFS:
                    dve.wait_ge(x_used, n - (SBUFS - 1))
                nc.vector.tensor_tensor(xl[0:k, s % SBUFS, 0:tiles, :], x[0:k, s % XBUF, 0:tiles, :],
                                        xh[0:k, s % SBUFS, 0:tiles, :].bitcast(F32), ALU.subtract).then_inc(xl_ready, 1)

            def w_low_part(c):
                if c < 0:
                    src, layer, t, tiles, k = w0a_st, 0, 0, TILES0, K0
                    dve.wait_ge(w_high, 1)
                else:
                    n = PREP.index((1, c))
                    src, layer, t, tiles, k = w_st[w_room(n)[0]], 1, c * CHUNK, CHUNK, K1
                    dve.wait_ge(w_high, n + 2)
                nc.vector.tensor_tensor(wl[layer][0:k, t:t + tiles, :], src[0:k],
                                        wh[layer][0:k, t:t + tiles, :].bitcast(F32), ALU.subtract).then_inc(w_low, 1)

            dve.wait_ge(w0_loaded, 32)
            nc.vector.tensor_tensor(w0a_st[0:K0], w0a_st[0:K0], w0b_st[0:K0], ALU.add).then_inc(w0_summed, 1)
            w_low_part(-1)
            for q in range(PAIRS0):
                multiply(0, q, 0, q, 0)
                if q:
                    low_part(0, q - 1, 0, q - 1)
            low_part(0, PAIRS0 - 1, 0, PAIRS0 - 1)
            for c in range(AHEAD):
                w_low_part(c)
            for q in range(PAIRS1):
                multiply(1, q, 0, PAIRS0 + q, 0)
                if q:
                    low_part(1, q - 1, 0, PAIRS0 + q - 1)
                if q in (6, 8):
                    w_low_part(AHEAD + (q - 6) // 2)

            ORDER = [(0, q, 1) for q in range(PAIRS0)] + [(2, q, 0) for q in range(PAIRS1)] + [(1, q, 1) for q in range(PAIRS1)]
            with dve.Fori(0, BLOCKS - 1) as i:
                for s, (layer, q, ahead) in enumerate(ORDER):
                    multiply(layer, q, i, LEAD + s, i + ahead)
                    before = ORDER[s - 1]
                    low_part(before[0], before[1], i, LEAD + s - 1)
            low_part(1, PAIRS1 - 1, BLOCKS - 1, LEAD - 1)
            for q in range(PAIRS1):
                multiply(2, q, BLOCKS - 1, LEAD + q, BLOCKS - 1)
                if q:
                    low_part(2, q - 1, BLOCKS - 1, LEAD + q - 1)
            low_part(2, PAIRS1 - 1, BLOCKS - 1, LEAD + PAIRS1 - 1)
            for part in range(2):
                dve.wait_ge(y2_last, part + 1)
                nc.vector.tensor_reduce(z[0:HALF, 2 + part, EARLY:BATCH],
                                        x[0:HALF, part, 0, :].rearrange("p (s d) -> p s d", d=DIM),
                                        mybir.AxisListType.X, ALU.add).then_inc(z_last, 1)

        @block.scalar
        def _(act):
            def high_part(layer, q, turn, s):
                t, tiles, k = stage_tiles(layer, q)
                n = turn * PAIRS + s
                act.wait_ge(x_ready, n + 1)
                if not isinstance(n, int) or n >= SBUFS:
                    act.wait_ge(x_used, n - (SBUFS - 1))
                nc.scalar.activation(xh[0:k, s % SBUFS, 0:tiles, :], x[0:k, s % XBUF, 0:tiles, :],
                                     ACT.Copy).then_inc(xh_ready, 1)

            def w_high_part(n):
                if n == 0:
                    src, layer, t, tiles, k = w0a_st, 0, 0, TILES0, K0
                    act.wait_ge(w0_summed, 1)
                else:
                    layer, c = PREP[n - 1]
                    src, t, tiles, k = w_st[w_room(n - 1)[0]], c * CHUNK, CHUNK, K1
                    act.wait_ge(w_loaded[w_room(n - 1)[0]], 16 * w_room(n - 1)[1])
                nc.scalar.activation(wh[layer][0:k, t:t + tiles, :], src[0:k], ACT.Copy).then_inc(w_high, 1)

            def hidden(layer, pairs):
                act.wait_ge(x_used, pairs)
                nc.scalar.activation(h[0:HALF, :], ps[0:HALF, 2 * layer, :], ACT.Relu,
                                     bias=bias_sb[:, 2 * layer:2 * layer + 1]).then_inc(h_made[layer], 1)

            def directs(layer, b, first, count):
                parts = (0, 1) if layer == 2 else (1,)
                total = len(parts) * BLOCK_B
                for n in range(first, min(first + count, total)):
                    part, sample = parts[n // BLOCK_B], n % BLOCK_B
                    y = ps[0:HALF, 2 * layer + part, sample * DIM:(sample + 1) * DIM]
                    ins = nc.scalar.activation(y, y, ACT.Relu, bias=bias_sb[:, 2 * layer + part:2 * layer + part + 1],
                                               accum_out=z[0:HALF, layer if layer < 2 else 2 + part,
                                                           bass.ds(b * BLOCK_B + sample, 1)])
                    if n == total - 1:
                        ins.then_inc(y_read, 1)

            for c in range(GATHERS):
                if GF * c < WRAP:
                    act.wait_ge(gathered0[c], 16)
                    write_rows(act, 0, c, FIELDS + GF * c, ROWS_E, scratch0_written)
            w_high_part(0)
            act.wait_ge(bias_loaded, 16)
            for q in range(PAIRS0):
                high_part(0, q, 0, q)
            for n in range(AHEAD):
                w_high_part(n + 1)
            hidden(0, PAIRS0)
            prepared = AHEAD + 1
            for q in range(PAIRS1):
                high_part(1, q, 0, PAIRS0 + q)
                if q >= HG and prepared <= len(PREP):
                    w_high_part(prepared)
                    prepared += 1
                directs(0, 0, q, 1)

            def turn(i):
                ORDER = [(0, q) for q in range(PAIRS0)] + [(2, q) for q in range(PAIRS1)] + [(1, q) for q in range(PAIRS1)]
                l1, l0, l2 = SBUFS - 1, PAIRS0 + HG - 1, PAIRS0 + PAIRS1 + SBUFS - 1
                for s, (layer, q) in enumerate(ORDER):
                    high_part(layer, q, i, LEAD + s)
                    if s == l1:
                        hidden(1, i * PAIRS + LEAD)
                    if s == l0:
                        hidden(0, i * PAIRS + (LEAD + PAIRS0))
                    if s == l2:
                        act.wait_ge(x_used, i * PAIRS + (LEAD + PAIRS0 + PAIRS1))
                    if l1 < s <= l1 + 8:
                        directs(1, i, 2 * (s - l1 - 1), 2)
                    elif l1 + 8 < s <= l1 + 16:
                        directs(0, i + 1, 2 * (s - l1 - 9), 2)
                    elif l2 < s <= l2 + 11:
                        directs(2, i, 3 * (s - l2 - 1), 3)

            with act.Fori(0, BLOCKS - 1) as i:
                turn(i)
            def hidden_top1(n, lo, hi):
                for m in range(H1T):
                    act.wait_ge(g1_sum, n * H1T + m + 1)
                    nc.scalar.activation(g1[m][:, lo:hi], ps[:, g1_bank(m), lo:hi], ACT.Relu,
                                         bias=bt1_sb[:, m:m + 1]).then_inc(g1_ready, 1)

            def hidden_top2(n, lo, hi):
                for m in range(H2T):
                    act.wait_ge(g2_sum, n * H2T + m + 1)
                    nc.scalar.activation(g2[m][:, lo:hi], ps[:, g2_bank(m), lo:hi], ACT.Relu,
                                         bias=bt2_sb[:, m:m + 1]).then_inc(g2_ready, 1)

            def output(n, lo, hi):
                act.wait_ge(out_sum, n + 1)
                nc.scalar.activation(y_sb[:, lo:hi], ps[0:1, OUT_BANK, lo:hi], ACT.Copy).then_inc(out_ready, 1)

            hidden(1, PAIRS * (BLOCKS - 1) + LEAD)
            hidden_top1(0, 0, EARLY)
            hidden_top2(0, 0, EARLY)
            for q in range(PAIRS1):
                high_part(2, q, BLOCKS - 1, LEAD + q)
                if q == HG - 1:
                    output(0, 0, EARLY)
                if q >= HG:
                    directs(1, BLOCKS - 1, 2 * (q - HG), 2)
            for part in range(2):
                act.wait_ge(x_used, PAIRS * BLOCKS)
                nc.scalar.activation(x[0:HALF, part, 0, :], ps[0:HALF, 4 + part, :], ACT.Relu,
                                     bias=bias_sb[:, 4 + part:5 + part]).then_inc(y2_last, 1)
            hidden_top1(1, EARLY, BATCH)
            hidden_top2(1, EARLY, BATCH)
            output(1, EARLY, BATCH)

        @block.tensor
        def _(pe):
            def contract(layer, q, turn, at):
                n, s = turn * PAIRS + at, at % SBUFS
                t0, tiles, k_ = stage_tiles(layer, q)
                total = TILES0 if layer == 0 else TILES1

                def mm(half, w, xs, a, start, stop):
                    t = t0 + a
                    return nc.tensor.matmul(ps[0:HALF, 2 * layer + half, :], w[layer][0:k_, t, half * HALF:(half + 1) * HALF],
                                            xs[0:k_, s, a, :], start=start, stop=stop)

                pe.wait_ge(xh_ready, n + 1)
                for a in range(tiles):
                    for half in range(2):
                        mm(half, wh, xh, a, t0 + a == 0, False)
                        mm(half, wl, xh, a, False, False)
                pe.wait_ge(xl_ready, n + 1)
                for a in range(tiles):
                    for half in range(2):
                        last = mm(half, wh, xl, a, False, t0 + a == total - 1)
                last.then_inc(x_used, 1)

            pe.wait_ge(w_low, 1)
            for q in range(PAIRS0):
                contract(0, q, 0, q)
            for q in range(PAIRS1):
                if q % 2 == 0:
                    pe.wait_ge(*w_split(1, q // 2))
                contract(1, q, 0, PAIRS0 + q)
            pe.wait_ge(*w_split(2, CHUNKS - 1))
            with pe.Fori(0, BLOCKS - 1) as i:
                pe.wait_ge(y_read, i * 3 + 1)
                for q in range(PAIRS0):
                    contract(0, q, i, LEAD + q)
                for q in range(PAIRS1):
                    contract(2, q, i, LEAD + PAIRS0 + q)
                pe.wait_ge(y_read, i * 3 + 2)
                for q in range(PAIRS1):
                    contract(1, q, i, LEAD + PAIRS0 + PAIRS1 + q)
            def tower(n, lo, hi):
                for cs in (range(0, 2), range(2, ZC)):
                    if n == 1 and cs[0] == 2:
                        pe.wait_ge(z_last, 2)
                    for m in range(H1T):
                        for c in cs:
                            last = nc.tensor.matmul(ps[:, g1_bank(m), lo:hi], wt1_sb[:, c, m * P:(m + 1) * P],
                                                    z[0:ZROWS, c, lo:hi], start=(c == 0), stop=(c == ZC - 1))
                        if cs[-1] == ZC - 1:
                            last.then_inc(g1_sum, 1)
                for m in range(H2T):
                    for k in range(H1T):
                        if m == 0:
                            pe.wait_ge(g1_ready, n * H1T + k + 1)
                        last = nc.tensor.matmul(ps[:, g2_bank(m), lo:hi], wt2_sb[:, k, m * P:(m + 1) * P],
                                                g1[k][:, lo:hi], start=(k == 0), stop=(k == H1T - 1))
                    last.then_inc(g2_sum, 1)
                for k in range(H2T):
                    pe.wait_ge(g2_ready, n * H2T + k + 1)
                    last = nc.tensor.matmul(ps[0:1, OUT_BANK, lo:hi], wt3_sb[:, k:k + 1], g2[k][:, lo:hi],
                                            start=(k == 0), stop=(k == H2T - 1))
                last.then_inc(out_sum, 1)

            pe.wait_ge(top_loaded, 16 * TOP_LOADS)
            pe.wait_ge(y_read, 3 * (BLOCKS - 1) + 1)
            pe.wait_ge(x_ready, PAIRS * (BLOCKS - 1) + LEAD)
            tower(0, 0, EARLY)
            for q in range(PAIRS1):
                contract(2, q, BLOCKS - 1, LEAD + q)
            pe.wait_ge(y_read, 3 * (BLOCKS - 1) + 2)
            tower(1, EARLY, BATCH)


def kernel(**inputs):
    import concourse.bacc as bacc
    from concourse.bass_utils import run_bass_kernel_spmd

    tables = [np.asarray(inputs[f"tbl_{f}"]) for f in range(FIELDS)]
    starts = np.concatenate([[0], np.cumsum([t.shape[0] for t in tables])[:-1]]).astype(np.int32)

    def lane(a, rows=P):
        return np.concatenate([a, np.zeros((rows - a.shape[0], *a.shape[1:]), a.dtype)]) if a.shape[0] < rows else a

    def cin_weights(w):
        w = np.asarray(w).reshape(MAPS, HG, GH, MP, 2, GM)
        return lane(np.ascontiguousarray(w.transpose(2, 5, 3, 1, 4, 0)).reshape(K1, TILES1, MAPS))

    w0 = np.asarray(inputs["L0_rec_W0"]).reshape(MAPS, FIELDS, FIELDS)
    near = np.zeros((DIST, FIELDS, TILES0, MAPS), w0.dtype)
    far = np.zeros((DIST, FIELDS, TILES0, MAPS), w0.dtype)
    for k in range(FIELDS // 2 + 1):
        for hh in range(FIELDS if k < FIELDS // 2 else FIELDS // 2):
            m = (hh + k) % FIELDS
            near[k % DIST, hh, k // DIST] = w0[:, hh, m]
            if k:
                far[k % DIST, hh, k // DIST] = w0[:, m, hh]

    def cols(v, n):
        return np.ascontiguousarray(np.asarray(v).reshape(n, -1).T)

    arrays = {
        "ids": np.ascontiguousarray(np.asarray(inputs["ids"]).reshape(BLOCKS, BLOCK_B, GATHERS, GF).transpose(3, 1, 0, 2)
                                    .reshape(P, BLOCKS * GATHERS)),
        "base": np.ascontiguousarray(np.repeat(starts.reshape(GATHERS, GF).T, BLOCK_B, axis=0)),
        "table": np.concatenate(tables),
        "w0a": lane(near.reshape(K0, TILES0, MAPS)),
        "w0b": lane(far.reshape(K0, TILES0, MAPS)),
        "w1": cin_weights(inputs["L0_rec_W1"]),
        "w2": cin_weights(inputs["L0_rec_W2"]),
        "bias": np.concatenate([cols(inputs[f"L0_rec_b{n}"], 2) for n in range(3)], axis=1),
        "wt1": np.ascontiguousarray(np.concatenate([
            np.asarray(inputs["W_top1"])[:ZC * HALF].reshape(ZC, HALF, -1).transpose(1, 0, 2),
            np.asarray(inputs["W_top1"])[ZC * HALF:].reshape(DENSE // ZC, ZC, -1)])),
        "bt1": cols(inputs["b_top1"], H1T),
        "wt2": np.asarray(inputs["W_top2"]),
        "bt2": cols(inputs["b_top2"], H2T),
        "wt3": cols(inputs["W_top3"], H2T),
        "dense": np.ascontiguousarray(np.asarray(inputs["dense_ctx"]).T),
    }
    nc = bacc.Bacc("TRN2", target_bir_lowering=False, num_devices=1)
    args = {k: nc.dram_tensor(f"in_{k}", a.shape, mybir.dt.from_np(a.dtype), kind="ExternalInput").ap()
            for k, a in arrays.items()}
    args["out"] = nc.dram_tensor("out_y", (1, BATCH), F32, kind="ExternalOutput").ap()
    args["scratch"] = nc.dram_tensor("scratch_e", (BLOCKS * ROWS_E, COLS), F32, kind="Internal").ap()
    build_tower(nc, **args)
    r = run_bass_kernel_spmd(nc, [{f"in_{k}": a for k, a in arrays.items()}], core_ids=[0])
    return r.results[0]["out_y"].reshape(BATCH, 1)
```
